# Optimizing a Trainium2 kernel written in Bass

```python
import numpy as np
import jax
import jax.numpy as jnp

def _softmax(x, axis=-1):
    return jax.nn.softmax(x, axis=axis)

def _gelu(x):
    return jax.nn.gelu(x, approximate=True)

def _silu(x):
    return jax.nn.silu(x)

def _sigmoid(x):
    return jax.nn.sigmoid(x)

def _layernorm(x, axis=-1, eps=1e-05):
    m = jnp.mean(x, axis=axis, keepdims=True)
    v = jnp.var(x, axis=axis, keepdims=True)
    return (x - m) / jnp.sqrt(v + eps)

def _scatter_add(tgt, idx, src, axis=0):
    return tgt.at[idx].add(src)

def _segment_sum(src, seg, n):
    return jax.ops.segment_sum(src, seg, n)
kernel_name = 'mk_dlrm_tower_d1_rec_r8_e07e4a'

def setup_inputs(seed: int=0):
    np.random.seed(seed)
    _w = jnp.asarray

    def _rec_inputs():
        import jax
        import jax.numpy as jnp
        _tk = jax.random.key(seed)
        dense_ctx = jax.random.normal(jax.random.fold_in(_tk, 190), (512, 16), jnp.float32)
        ids = jnp.stack([jax.random.randint(jax.random.fold_in(_tk, 200 + f), (512,), 0, v, jnp.int32) for f, v in enumerate([1250, 12500, 1250, 1250, 1000, 1000, 1000, 12500, 12500, 125000, 1000, 1250, 12500, 12500, 1000, 1250, 12500, 1250, 1000, 1250, 12500, 12500, 1000, 1000, 1000, 1250, 1250])], axis=1)
        tbl_0 = 0.05 * jax.random.normal(jax.random.fold_in(_tk, 500 + 0), (1250, 128), jnp.float32)
        tbl_1 = 0.05 * jax.random.normal(jax.random.fold_in(_tk, 500 + 1), (12500, 128), jnp.float32)
        tbl_2 = 0.05 * jax.random.normal(jax.random.fold_in(_tk, 500 + 2), (1250, 128), jnp.float32)
        tbl_3 = 0.05 * jax.random.normal(jax.random.fold_in(_tk, 500 + 3), (1250, 128), jnp.float32)
        tbl_4 = 0.05 * jax.random.normal(jax.random.fold_in(_tk, 500 + 4), (1000, 128), jnp.float32)
        tbl_5 = 0.05 * jax.random.normal(jax.random.fold_in(_tk, 500 + 5), (1000, 128), jnp.float32)
        tbl_6 = 0.05 * jax.random.normal(jax.random.fold_in(_tk, 500 + 6), (1000, 128), jnp.float32)
        tbl_7 = 0.05 * jax.random.normal(jax.random.fold_in(_tk, 500 + 7), (12500, 128), jnp.float32)
        tbl_8 = 0.05 * jax.random.normal(jax.random.fold_in(_tk, 500 + 8), (12500, 128), jnp.float32)
        tbl_9 = 0.05 * jax.random.normal(jax.random.fold_in(_tk, 500 + 9), (125000, 128), jnp.float32)
        tbl_10 = 0.05 * jax.random.normal(jax.random.fold_in(_tk, 500 + 10), (1000, 128), jnp.float32)
        tbl_11 = 0.05 * jax.random.normal(jax.random.fold_in(_tk, 500 + 11), (1250, 128), jnp.float32)
        tbl_12 = 0.05 * jax.random.normal(jax.random.fold_in(_tk, 500 + 12), (12500, 128), jnp.float32)
        tbl_13 = 0.05 * jax.random.normal(jax.random.fold_in(_tk, 500 + 13), (12500, 128), jnp.float32)
        tbl_14 = 0.05 * jax.random.normal(jax.random.fold_in(_tk, 500 + 14), (1000, 128), jnp.float32)
        tbl_15 = 0.05 * jax.random.normal(jax.random.fold_in(_tk, 500 + 15), (1250, 128), jnp.float32)
        tbl_16 = 0.05 * jax.random.normal(jax.random.fold_in(_tk, 500 + 16), (12500, 128), jnp.float32)
        tbl_17 = 0.05 * jax.random.normal(jax.random.fold_in(_tk, 500 + 17), (1250, 128), jnp.float32)
        tbl_18 = 0.05 * jax.random.normal(jax.random.fold_in(_tk, 500 + 18), (1000, 128), jnp.float32)
        tbl_19 = 0.05 * jax.random.normal(jax.random.fold_in(_tk, 500 + 19), (1250, 128), jnp.float32)
        tbl_20 = 0.05 * jax.random.normal(jax.random.fold_in(_tk, 500 + 20), (12500, 128), jnp.float32)
        tbl_21 = 0.05 * jax.random.normal(jax.random.fold_in(_tk, 500 + 21), (12500, 128), jnp.float32)
        tbl_22 = 0.05 * jax.random.normal(jax.random.fold_in(_tk, 500 + 22), (1000, 128), jnp.float32)
        tbl_23 = 0.05 * jax.random.normal(jax.random.fold_in(_tk, 500 + 23), (1000, 128), jnp.float32)
        tbl_24 = 0.05 * jax.random.normal(jax.random.fold_in(_tk, 500 + 24), (1000, 128), jnp.float32)
        tbl_25 = 0.05 * jax.random.normal(jax.random.fold_in(_tk, 500 + 25), (1250, 128), jnp.float32)
        tbl_26 = 0.05 * jax.random.normal(jax.random.fold_in(_tk, 500 + 26), (1250, 128), jnp.float32)
        _rk = jax.random.fold_in(_tk, 7)
        W_top1 = 0.0521996 * jax.random.normal(jax.random.fold_in(_tk, 801), (367, 512), jnp.float32)
        W_top2 = 0.0441942 * jax.random.normal(jax.random.fold_in(_tk, 802), (512, 256), jnp.float32)
        W_top3 = 0.0625 * jax.random.normal(jax.random.fold_in(_tk, 803), (256, 1), jnp.float32)
        b_top1 = jnp.zeros((512,), jnp.float32)
        b_top2 = jnp.zeros((256,), jnp.float32)
        return (dense_ctx, ids, tbl_0, tbl_1, tbl_2, tbl_3, tbl_4, tbl_5, tbl_6, tbl_7, tbl_8, tbl_9, tbl_10, tbl_11, tbl_12, tbl_13, tbl_14, tbl_15, tbl_16, tbl_17, tbl_18, tbl_19, tbl_20, tbl_21, tbl_22, tbl_23, tbl_24, tbl_25, tbl_26, W_top1, b_top1, W_top2, b_top2, W_top3)
    dense_ctx, ids, tbl_0, tbl_1, tbl_2, tbl_3, tbl_4, tbl_5, tbl_6, tbl_7, tbl_8, tbl_9, tbl_10, tbl_11, tbl_12, tbl_13, tbl_14, tbl_15, tbl_16, tbl_17, tbl_18, tbl_19, tbl_20, tbl_21, tbl_22, tbl_23, tbl_24, tbl_25, tbl_26, W_top1, b_top1, W_top2, b_top2, W_top3 = _rec_inputs()

    def _L0_rec_setup():
        import jax, jax.numpy as jnp
        import numpy as np
        key = jax.random.key(seed)
        B, F, D = (2048, 27, 128)
        inputs = jax.random.normal(key, (B, F, D), dtype=jnp.float32)
        return {'inputs': inputs, 'num_feas': F}
    _L0_rec_all = _L0_rec_setup()
    _L0_rec_in = {k: v for k, v in _L0_rec_all.items() if k in ()}
    del _L0_rec_all
    return {'dense_ctx': dense_ctx, 'ids': ids, 'tbl_0': tbl_0, 'tbl_1': tbl_1, 'tbl_2': tbl_2, 'tbl_3': tbl_3, 'tbl_4': tbl_4, 'tbl_5': tbl_5, 'tbl_6': tbl_6, 'tbl_7': tbl_7, 'tbl_8': tbl_8, 'tbl_9': tbl_9, 'tbl_10': tbl_10, 'tbl_11': tbl_11, 'tbl_12': tbl_12, 'tbl_13': tbl_13, 'tbl_14': tbl_14, 'tbl_15': tbl_15, 'tbl_16': tbl_16, 'tbl_17': tbl_17, 'tbl_18': tbl_18, 'tbl_19': tbl_19, 'tbl_20': tbl_20, 'tbl_21': tbl_21, 'tbl_22': tbl_22, 'tbl_23': tbl_23, 'tbl_24': tbl_24, 'tbl_25': tbl_25, 'tbl_26': tbl_26, 'W_top1': W_top1, 'b_top1': b_top1, 'W_top2': W_top2, 'b_top2': b_top2, 'W_top3': W_top3}

def reference(dense_ctx, ids, tbl_0, tbl_1, tbl_2, tbl_3, tbl_4, tbl_5, tbl_6, tbl_7, tbl_8, tbl_9, tbl_10, tbl_11, tbl_12, tbl_13, tbl_14, tbl_15, tbl_16, tbl_17, tbl_18, tbl_19, tbl_20, tbl_21, tbl_22, tbl_23, tbl_24, tbl_25, tbl_26, W_top1, b_top1, W_top2, b_top2, W_top3):
    import jax
    import jax.numpy as jnp

    def _L0_rec_ref(inputs, num_feas):
        import jax, jax.numpy as jnp
        import numpy as np
        dot_products = jnp.einsum('bnd,bmd->bnm', inputs, inputs)
        r, c = np.tril_indices(num_feas, k=-1)
        flat_interactions = dot_products[:, c, r]
        return flat_interactions
    e = jnp.stack([tbl_0[ids[:, 0]], tbl_1[ids[:, 1]], tbl_2[ids[:, 2]], tbl_3[ids[:, 3]], tbl_4[ids[:, 4]], tbl_5[ids[:, 5]], tbl_6[ids[:, 6]], tbl_7[ids[:, 7]], tbl_8[ids[:, 8]], tbl_9[ids[:, 9]], tbl_10[ids[:, 10]], tbl_11[ids[:, 11]], tbl_12[ids[:, 12]], tbl_13[ids[:, 13]], tbl_14[ids[:, 14]], tbl_15[ids[:, 15]], tbl_16[ids[:, 16]], tbl_17[ids[:, 17]], tbl_18[ids[:, 18]], tbl_19[ids[:, 19]], tbl_20[ids[:, 20]], tbl_21[ids[:, 21]], tbl_22[ids[:, 22]], tbl_23[ids[:, 23]], tbl_24[ids[:, 24]], tbl_25[ids[:, 25]], tbl_26[ids[:, 26]]], axis=1)
    z = _L0_rec_ref(e, 27)
    z = z.reshape(z.shape[0], -1)
    h = jnp.concatenate([z, dense_ctx], axis=1)
    h = jnp.maximum(h @ W_top1 + b_top1, 0.0)
    h = jnp.maximum(h @ W_top2 + b_top2, 0.0)
    y = h @ W_top3
    return y

_drawn_inputs = setup_inputs


def setup_inputs(seed=0):
    import zlib

    import numpy as np

    out = dict(_drawn_inputs(seed))
    spreads = {'b_top1': (0.0, 0.1), 'b_top2': (0.0, 0.1)}
    factors = {}
    for name, (base, spread) in spreads.items():
        noise = np.random.default_rng([zlib.crc32(name.encode()), seed]).standard_normal(out[name].shape)
        drawn = base * np.exp(spread * noise) if base else spread * noise
        out[name] = jnp.asarray(drawn.astype(out[name].dtype))
    for name, factor in factors.items():
        out[name] = (out[name] * factor).astype(out[name].dtype)
    return out
```

```python
import numpy as np
import concourse.bass as bass
from concourse import mybir
from contextlib import ExitStack

B = 512
F = 27
D = 128
ND = 16
H1, H2 = 512, 256
P = 128
T = B // P
SLOT = 32
GS = P // SLOT
GROUPS = P // GS
UNIT = 8
UNITS = GROUPS // UNIT
Q = P // SLOT
K1 = 7
BANK = 512

ROWS_OH = 1000
CH = 8
CR = ROWS_OH // CH
ONEHOT = [4, 5, 6, 10, 14, 18]
X = len(ONEHOT)
NT = 4
GATHERED = [f for f in range(F) if f not in ONEHOT]
NGF = len(GATHERED)
ORDER = ONEHOT + GATHERED
TG = [(a, min(a + 4, NGF)) for a in range(0, NGF, 4)]
NTG = len(TG)
MC = H1 // P
MC2 = H2 // P


def tower(nc, ids, ids_t, dense_t, tbls, w1, w2, cols, y):
    fp32 = mybir.dt.float32
    i32 = mybir.dt.int32
    ALU = mybir.AluOpType
    ACT = mybir.ActivationFunctionType

    with ExitStack() as ctx:
        def sb(name, shape, dt=fp32):
            return ctx.enter_context(nc.sbuf_tensor(name, shape, dt))

        def pb(name, shape):
            return ctx.enter_context(nc.psum_tensor(name, shape, fp32))

        def sem(name):
            return ctx.enter_context(nc.semaphore(name))

        ids_sb = sb("ids_sb", [P, T, F], i32)
        ids_bc = sb("ids_bc", [CR, X, B], i32)
        tbl_sb = sb("tbl_sb", [CR, NT, CH * D])
        onehot = sb("onehot", [CR, 2, CH, B])
        row_i = sb("row_i", [P, CH], i32)
        row_no = sb("row_no", [P, CH])
        emb = sb("emb", [P, T, NGF, D])
        embT = sb("embT", [P, T, P, SLOT])
        ident = sb("ident", [P, P])
        dots = sb("dots", [P, T, K1, P])
        w1_sb = sb("w1_sb", [P, K1, H1])
        w2_sb = sb("w2_sb", [P, MC, H2])
        cols_sb = sb("cols_sb", [P, MC + 2 * MC2])
        b1_sb = cols_sb[:, 0:MC]
        b2_sb = cols_sb[:, MC:MC + MC2]
        w3_sb = cols_sb[:, MC + MC2:MC + 2 * MC2]
        h1 = sb("h1", [P, MC, P])
        h2 = sb("h2", [P, MC2, P])
        y_sb = sb("y_sb", [1, B])

        tp = pb("tp", [P, 2, BANK])
        gram = [pb(f"gram{i}", [P, 2, BANK]) for i in range(2)]
        half = [pb(f"half{i}", [P, 4, P]) for i in range(2)]

        s_ids = sem("s_ids")
        s_idsbc = sem("s_idsbc")
        s_tbl = [sem(f"s_tbl{n}") for n in range(X)]
        s_w1 = sem("s_w1")
        s_wr = sem("s_wr")
        s_dense = sem("s_dense")
        s_rowi = sem("s_rowi")
        s_row = sem("s_row")
        s_id0 = sem("s_id0")
        s_ident = sem("s_ident")
        s_zero = sem("s_zero")
        s_oh = sem("s_oh")
        s_gat = [[sem(f"s_gat{t}_{g}") for g in range(NTG)] for t in range(T)]
        s_tp = sem("s_tp")
        s_tpfree = sem("s_tpfree")
        s_embA = sem("s_embA")
        s_gram = sem("s_gram")
        s_dotsa = sem("s_dotsa")
        s_dotsv = sem("s_dotsv")
        s_ps1 = sem("s_ps1")
        s_h1a = sem("s_h1a")
        s_h1v = sem("s_h1v")
        s_ps2 = sem("s_ps2")
        s_h2a = sem("s_h2a")
        s_h2v = sem("s_h2v")
        s_ps3 = sem("s_ps3")
        s_y = sem("s_y")
        s_out = sem("s_out")

        block = ctx.enter_context(nc.Block())

        fills = []
        for n in range(X):
            fills.append(("oh", n))
            if n == 2:
                fills += [("tp", 0, g) for g in range(NTG)]
        for t in range(1, T):
            fills += [("tp", t, g) for g in range(NTG)]
        fill_no = {w: i for i, w in enumerate(fills)}

        @block.sync
        def _(sp):
            sp.dma_start(ids_sb[:], ids.rearrange("(t p) f -> p t f", p=P)).then_inc(s_ids, 16)
            for n, f in enumerate(ONEHOT):
                sp.dma_start(ids_bc[:, n, :], ids_t[f:f + 1, :].broadcast_to([CR, B])).then_inc(s_idsbc, 16)
            for n, f in enumerate(ONEHOT):
                if n >= NT:
                    sp.wait_ge(s_tp, fill_no[("oh", n - NT)] + 1)
                sp.dma_start(tbl_sb[:, n % NT, :], tbls[f].rearrange("(p c) d -> p (c d)", c=CH)).then_inc(s_tbl[n], 16)
            sp.wait_ge(s_y, T)
            sp.dma_start(y, y_sb[:, :]).then_inc(s_out, 16)
            sp.wait_ge(s_out, 16)

        @block.gpsimd
        def _(pool):
            nc.gpsimd.iota(row_i[:], pattern=[[1, CH]], base=0, channel_multiplier=CH).then_inc(s_rowi, 1)
            nc.gpsimd.memset(ident[:], 0.0).then_inc(s_id0, 1)
            pool.wait_ge(s_id0, 1)
            nc.gpsimd.affine_select(out=ident[:], in_=ident[:], compare_op=ALU.not_equal, fill=1.0, base=0,
                                    pattern=[[-1, P]], channel_multiplier=1).then_inc(s_ident, 1)
            pool.wait_ge(s_ids, 16)
            for t in range(T):
                for g, (a, e) in enumerate(TG):
                    for n in range(a, e):
                        f = GATHERED[n]
                        nc.gpsimd.indirect_dma_start(
                            out=emb[:, t, n, :], out_offset=None, in_=tbls[f],
                            in_offset=bass.IndirectOffsetOnAxis(ap=ids_sb[:, t, f:f + 1], axis=0),
                        ).then_inc(s_gat[t][g], 16)

        def evac_fill(eng, copy, what):
            i = fill_no[what]
            eng.wait_ge(s_tp, i + 1)
            if what[0] == "oh":
                n = what[1]
                copy(embT[:, :, :, n].rearrange("p t b -> p (t b)"), tp[:, i % 2, :]).then_inc(s_tpfree if i % 2 == 0 else s_embA, 1)
            else:
                _, t, g = what
                a, e = TG[g]
                copy(embT[:, t, :, X + a:X + e],
                     tp[:, i % 2, 0:(e - a) * P].rearrange("p (f b) -> p b f", f=e - a)).then_inc(
                         s_tpfree if i % 2 == 0 else s_embA, 1)

        def evac_unit(eng, copy, t, u, samples, final):
            i = t * UNITS + u
            eng.wait_ge(s_gram, i + 1)
            for s in samples:
                for q in range(Q):
                    nk = min(K1, F - 1 - K1 * q)
                    src = gram[i % 2][SLOT * s:SLOT * s + F, :, 0:4 * GS * F].rearrange(
                        "p h (g s j) -> p h g s j", g=4, s=GS)[:, :, :, s, K1 * q:K1 * q + nk]
                    dst = dots[SLOT * q:SLOT * q + F, t, 0:nk, :].rearrange(
                        "p k (u h g s) -> p u h g s k", u=UNITS, h=2, g=4)[:, u, :, :, s, :]
                    last = copy(dst, src)
            last.then_inc(final, 1)

        @block.vector
        def _(dve):
            nc.vector.memset(dots[:], 0.0).then_inc(s_zero, 1)
            nc.vector.memset(embT[:, :, :, F:SLOT].rearrange("p t b s -> p (t b) s"), 0.0).then_inc(s_zero, 1)
            dve.wait_ge(s_rowi, 1)
            nc.vector.tensor_copy(row_no[:], row_i[:]).then_inc(s_row, 1)
            dve.wait_ge(s_row, 1)
            dve.wait_ge(s_zero, 2)
            dve.wait_ge(s_idsbc, 16 * X)

            def make_onehot(n):
                if n >= 2:
                    dve.wait_ge(s_tp, fill_no[("oh", n - 2)] + 1)
                for c in range(CH):
                    nc.vector.tensor_scalar(onehot[:, n % 2, c, :], ids_bc[:, n, :], row_no[0:CR, c:c + 1], None,
                                            ALU.is_equal).then_inc(s_oh, 1)
            made = 0
            for i, what in enumerate(fills):
                if what[0] == "oh":
                    while made < min(X, what[1] + 2):
                        make_onehot(made)
                        made += 1
                elif what[1] > 0:
                    break
                if i % 2 == 0:
                    evac_fill(dve, nc.vector.tensor_copy, what)
            for t in range(T):
                if t > 0:
                    for g in range(NTG):
                        if fill_no[("tp", t, g)] % 2 == 0:
                            evac_fill(dve, nc.vector.tensor_copy, ("tp", t, g))
                for u in range(UNITS):
                    evac_unit(dve, nc.vector.tensor_copy, t, u, (2, 3), s_dotsv)
                dve.wait_ge(s_ps1, t * 2 + 2)
                for m in (2, 3):
                    nc.vector.tensor_scalar(h1[:, m, :], half[1][:, m - 2, :], b1_sb[:, m:m + 1], 0.0, ALU.add,
                                            ALU.max).then_inc(s_h1v, 1)
                dve.wait_ge(s_ps2, t * MC2 + 2)
                nc.vector.tensor_scalar(h2[:, 1, :], half[1][:, 2, :], b2_sb[:, 1:2], 0.0, ALU.add,
                                        ALU.max).then_inc(s_h2v, 1)
                dve.wait_ge(s_ps3, t + 1)
                nc.vector.tensor_copy(y_sb[:, t * P:(t + 1) * P], half[0][0:1, 3, :]).then_inc(s_y, 1)

        @block.scalar
        def _(act):
            act.dma_start(w1_sb[:], w1).then_inc(s_w1, 16)
            act.dma_start(w2_sb[:], w2.rearrange("(c p) n -> p c n", p=P)).then_inc(s_wr, 16)
            act.dma_start(cols_sb[:], cols).then_inc(s_wr, 16)
            act.wait_ge(s_zero, 2)
            act.dma_start(dots[3 * SLOT:3 * SLOT + ND, :, K1 - 1, :],
                          dense_t.rearrange("n (t b) -> n t b", t=T)).then_inc(s_dense, 16)
            for i, what in enumerate(fills):
                if what[0] == "tp" and what[1] > 0:
                    break
                if i % 2 == 1:
                    evac_fill(act, nc.scalar.copy, what)
            act.wait_ge(s_wr, 32)
            for t in range(T):
                if t > 0:
                    for g in range(NTG):
                        if fill_no[("tp", t, g)] % 2 == 1:
                            evac_fill(act, nc.scalar.copy, ("tp", t, g))
                for u in range(UNITS):
                    evac_unit(act, nc.scalar.copy, t, u, (0, 1), s_dotsa)
                act.wait_ge(s_ps1, t * 2 + 1)
                for m in (0, 1):
                    nc.scalar.activation(h1[:, m, :], half[0][:, m, :], ACT.Relu, bias=b1_sb[:, m:m + 1]).then_inc(s_h1a, 1)
                act.wait_ge(s_ps2, t * MC2 + 1)
                nc.scalar.activation(h2[:, 0, :], half[0][:, 2, :], ACT.Relu, bias=b2_sb[:, 0:1]).then_inc(s_h2a, 1)

        @block.tensor
        def _(pe):
            def tp_free(i):
                if i >= 2:
                    pe.wait_ge(s_tpfree if i % 2 == 0 else s_embA, i // 2)

            def one_hot(n):
                i = fill_no[("oh", n)]
                tp_free(i)
                pe.wait_ge(s_tbl[n], 16)
                for c in range(CH):
                    pe.wait_ge(s_oh, n * CH + c + 1)
                    last = nc.tensor.matmul(tp[:, i % 2, :], tbl_sb[:, n % NT, c * D:(c + 1) * D], onehot[:, n % 2, c, :],
                                            start=(c == 0), stop=(c == CH - 1))
                last.then_inc(s_tp, 1)

            def transposes(t, g):
                i = fill_no[("tp", t, g)]
                tp_free(i)
                a, e = TG[g]
                pe.wait_ge(s_gat[t][g], 16 * (e - a))
                for n in range(a, e):
                    last = nc.tensor.transpose(tp[:, i % 2, (n - a) * P:(n - a + 1) * P], emb[:, t, n, :], ident[:])
                last.then_inc(s_tp, 1)

            pe.wait_ge(s_ident, 1)
            for what in fills:
                if what[0] == "oh":
                    one_hot(what[1])
                elif what[1] == 0:
                    transposes(0, what[2])
            for t in range(T):
                if t > 0:
                    for g in range(NTG):
                        transposes(t, g)
                n_even = (fill_no[("tp", t, NTG - 1)] + 2) // 2
                n_odd = (fill_no[("tp", t, NTG - 1)] + 1) // 2
                if t == 0:
                    n_even = (fill_no[("oh", X - 1)] + 2) // 2
                    n_odd = (fill_no[("oh", X - 1)] + 1) // 2
                    pe.wait_ge(s_zero, 2)
                pe.wait_ge(s_tpfree, n_even)
                pe.wait_ge(s_embA, n_odd)
                for u in range(UNITS):
                    i = t * UNITS + u
                    if i >= 2:
                        pe.wait_ge(s_dotsa, i - 1)
                        pe.wait_ge(s_dotsv, i - 1)
                    for g in range(UNIT):
                        b0 = (u * UNIT + g) * GS
                        last = nc.tensor.matmul(gram[i % 2][:, g // 4, (g % 4) * GS * F:(g % 4 + 1) * GS * F],
                                                embT[:, t, b0:b0 + GS, :].rearrange("p b s -> p (b s)"),
                                                embT[:, t, b0:b0 + GS, 0:F],
                                                start=True, stop=True)
                    last.then_inc(s_gram, 1)
                if t == 0:
                    pe.wait_ge(s_w1, 16)
                    pe.wait_ge(s_wr, 32)
                    pe.wait_ge(s_dense, 16)
                pe.wait_ge(s_dotsa, UNITS * (t + 1))
                pe.wait_ge(s_dotsv, UNITS * (t + 1))
                if t > 0:
                    pe.wait_ge(s_y, t)
                for m in range(MC):
                    for k in range(K1):
                        last = nc.tensor.matmul(half[m // 2][:, m % 2, :], w1_sb[:, k, m * P:(m + 1) * P], dots[:, t, k, :],
                                                start=(k == 0), stop=(k == K1 - 1))
                    if m % 2 == 1:
                        last.then_inc(s_ps1, 1)
                for m2 in range(MC2):
                    for m in range(MC):
                        pe.wait_ge(s_h1a if m < 2 else s_h1v, 2 * t + 2)
                        last = nc.tensor.matmul(half[m2][:, 2, :], w2_sb[:, m, m2 * P:(m2 + 1) * P],
                                                h1[:, m, :], start=(m == 0), stop=(m == MC - 1))
                    last.then_inc(s_ps2, 1)
                for m2 in range(MC2):
                    pe.wait_ge(s_h2a if m2 == 0 else s_h2v, t + 1)
                    last = nc.tensor.matmul(half[0][0:1, 3, :], w3_sb[:, m2:m2 + 1], h2[:, m2, :],
                                            start=(m2 == 0), stop=(m2 == MC2 - 1))
                last.then_inc(s_ps3, 1)


def kernel(**inputs):
    import concourse.bacc as bacc
    from concourse.bass_utils import run_bass_kernel_spmd as run

    nc = bacc.Bacc("TRN2", target_bir_lowering=False, num_devices=1)
    arrays = {}

    def give(name, a):
        a = np.ascontiguousarray(a)
        arrays[name] = a
        return nc.dram_tensor(name, a.shape, mybir.dt.from_np(a.dtype), kind="ExternalInput").ap()

    w_top1 = np.asarray(inputs["W_top1"])
    w1 = np.zeros((P, K1, H1), w_top1.dtype)
    for j in range(F - 1):
        for i in range(j + 1, F):
            hi, lo = max(ORDER[i], ORDER[j]), min(ORDER[i], ORDER[j])
            w1[SLOT * (j // K1) + i, j % K1] = w_top1[hi * (hi - 1) // 2 + lo]
    w1[3 * SLOT:3 * SLOT + ND, K1 - 1] = w_top1[F * (F - 1) // 2:]

    ids = give("ids_dram", inputs["ids"])
    ids_t = give("ids_t_dram", np.asarray(inputs["ids"]).T)
    dense_t = give("dense_t_dram", np.asarray(inputs["dense_ctx"]).T)
    tbls = [give(f"tbl_{f}_dram", inputs[f"tbl_{f}"]) for f in range(F)]
    w1 = give("w1_dram", w1)
    w2 = give("w2_dram", inputs["W_top2"])
    columns = [np.asarray(inputs[n]).reshape(-1, P) for n in ("b_top1", "b_top2", "W_top3")]
    cols = give("cols_dram", np.concatenate(columns).T)
    y = nc.dram_tensor("y_dram", (B, 1), mybir.dt.float32, kind="ExternalOutput").ap()
    tower(nc, ids, ids_t, dense_t, tbls, w1, w2, cols, y.rearrange("b o -> o b"))
    r = run(nc, [arrays], core_ids=[0])
    return r.results[0]["y_dram"]
```

```python
import numpy as np
import concourse.bass as bass
from concourse import mybir
from contextlib import ExitStack

B = 512
F = 27
D = 128
ND = 16
H1, H2 = 512, 256
P = 128
T = B // P
SLOT = 32
GS = P // SLOT
GROUPS = P // GS
UNIT = 8
UNITS = GROUPS // UNIT
US = UNIT * GS
Q = P // SLOT
BANK = 512

HALF = (F - 1) // 2
MERGED = HALF + 1
K1 = -(-MERGED // Q)
DENSE_Q, DENSE_K = Q - 1, MERGED - K1 * (Q - 1)

ROWS_OH = 1000
CH = 8
CR = ROWS_OH // CH
ONEHOT = [4, 5, 6, 10, 14, 18, 22]
X = len(ONEHOT)
NT = 3
GATHERED = [f for f in range(F) if f not in ONEHOT]
NG = len(GATHERED)
ORDER = ONEHOT + GATHERED
TRANS = 4
TG = [(a, min(a + TRANS, NG)) for a in range(0, NG, TRANS)]
NTG = len(TG)
MC = H1 // P
MC2 = H2 // P


BETWEEN = [0, 3, 1, 1, 2, 1, 2]
assert len(BETWEEN) == X and sum(BETWEEN) == 2 * NTG


def fill_order():
    early = [("tr", t, g) for t in (0, 1) for g in range(NTG)]
    order = []
    for n in range(X):
        order.append(("oh", n))
        order += early[:BETWEEN[n]]
        early = early[BETWEEN[n]:]
    return order + [("tr", t, g) for t in range(2, T) for g in range(NTG)]


def tower(nc, ids, ids_t, dense_t, tbls, w1, w2, cols, pick, y):
    fp32, bf16, i32, i16, u16 = (mybir.dt.float32, mybir.dt.bfloat16, mybir.dt.int32, mybir.dt.int16,
                                 mybir.dt.uint16)
    ALU = mybir.AluOpType
    ACT = mybir.ActivationFunctionType

    FILLS = fill_order()
    FILL_NO = {w: i for i, w in enumerate(FILLS)}
    EARLY = [w for w in FILLS if w[0] == "oh" or w[1] < 2]

    def taker(i):
        return "act" if i < len(EARLY) or i % 2 else "dve"

    def taken_of(i):
        return sum(taker(j) == taker(i) for j in range(i + 1))

    with ExitStack() as ctx:
        def sb(name, shape, dt=fp32):
            return ctx.enter_context(nc.sbuf_tensor(name, shape, dt))

        def pb(name, shape):
            return ctx.enter_context(nc.psum_tensor(name, shape, fp32))

        def sem(name):
            return ctx.enter_context(nc.semaphore(name))

        ids_sb = sb("ids_sb", [P, T, F], i32)
        ids_bc = sb("ids_bc", [CR, X, B], i32)
        ids_16 = sb("ids_16", [CR, X, B], i16)
        table = sb("table", [CR, NT, CH * D])
        rest = sb("rest", [CR, 2, CH * D])
        low = sb("low", [CR, 2, CH * D], bf16)
        onehot = sb("onehot", [CR, 2, CH, B], bf16)
        row_int = sb("row_int", [P, CH], i32)
        row_no = sb("row_no", [P, CH])
        emb = sb("emb", [P, T, NG, D])
        embT = sb("embT", [P, T, P, SLOT])
        ident = sb("ident", [P, P], bf16)
        dots = sb("dots", [P, T, 2, K1, P])
        pick_sb = sb("pick_sb", [P, K1], i32)
        w1_sb = sb("w1_sb", [P, K1, H1])
        w2_sb = sb("w2_sb", [P, MC, H2])
        cols_sb = sb("cols_sb", [P, MC + 2 * MC2])
        b1_sb = cols_sb[:, 0:MC]
        b2_sb = cols_sb[:, MC:MC + MC2]
        w3_sb = cols_sb[:, MC + MC2:MC + 2 * MC2]
        h1 = sb("h1", [P, MC, 2 * P])
        h2 = sb("h2", [P, MC2, 2 * P])
        y_sb = sb("y_sb", [1, B])

        fill = pb("fill", [P, 2, BANK])
        gram = [pb(f"gram{i}", [P, UNIT, P]) for i in range(2)]
        layer = [pb(f"layer{i}", [P, BANK]) for i in range(2)]

        emb_h = emb[:].bitcast(bf16).rearrange("p t n (d h) -> p t n h d", h=2)
        fill_h = fill[:].bitcast(bf16).rearrange("p i (n h b) -> p i n h b", h=2, b=P)
        fill_u = fill[:].bitcast(u16).rearrange("p i (n h b) -> p i b n h", h=2, b=P)
        table_hi = table[:].bitcast(bf16).rearrange("p n (c d h) -> p n c h d", h=2, d=D)[:, :, :, 1, :]
        rest_hi = rest[:].bitcast(bf16).rearrange("p n (c d h) -> p n c h d", h=2, d=D)[:, :, :, 1, :]
        low_c = low[:].rearrange("p n (c d) -> p n c d", d=D)
        embT_u = embT[:].bitcast(u16).rearrange("p t b (s h) -> p t b s h", h=2)

        ids_in = sem("ids_in")
        idsbc_in = [sem(f"idsbc_in{n}") for n in range(X)]
        table_in = [sem(f"table_in{n}") for n in range(X)]
        w1_in = sem("w1_in")
        rest_in = sem("rest_in")
        dense_in = sem("dense_in")
        gathered = [[sem(f"gathered{t}_{g}") for g in range(NTG)] for t in range(T)]
        row_made = sem("row_made")
        row_ready = sem("row_ready")
        ident_zero = sem("ident_zero")
        ident_ready = sem("ident_ready")
        zeros_ready = sem("zeros_ready")
        ids16_ready = sem("ids16_ready")
        onehot_ready = sem("onehot_ready")
        rest_ready = sem("rest_ready")
        low_ready = sem("low_ready")
        filled = sem("filled")
        taken_v = sem("taken_v")
        taken_a = sem("taken_a")
        gram_ready = sem("gram_ready")
        dots_a = sem("dots_a")
        dots_v = sem("dots_v")
        merged = sem("merged")
        layer1_ready = sem("layer1_ready")
        h1_a = sem("h1_a")
        h1_v = sem("h1_v")
        layer2_ready = sem("layer2_ready")
        h2_a = sem("h2_a")
        h2_v = sem("h2_v")
        layer3_ready = sem("layer3_ready")
        y_ready = sem("y_ready")
        y_out = sem("y_out")

        block = ctx.enter_context(nc.Block())

        @block.sync
        def _(sp):
            sp.dma_start(ids_sb[:], ids.rearrange("(t p) f -> p t f", p=P)).then_inc(ids_in, 16)
            for n, f in enumerate(ONEHOT):
                if n == NT:
                    sp.dma_start(w1_sb[:], w1).then_inc(w1_in, 16)
                if n >= NT:
                    sp.wait_ge(filled, FILL_NO[("oh", n - NT)] + 1)
                sp.dma_start(ids_bc[:, n, :], ids_t[f:f + 1, :].broadcast_to([CR, B])).then_inc(idsbc_in[n], 16)
                sp.dma_start(table[:, n % NT, :], tbls[f].rearrange("(p c) d -> p (c d)", c=CH)).then_inc(
                    table_in[n], 16)
            sp.dma_start(w2_sb[:], w2.rearrange("(c p) n -> p c n", p=P)).then_inc(rest_in, 16)
            sp.dma_start(cols_sb[:], cols).then_inc(rest_in, 16)
            sp.dma_start(pick_sb[:], pick).then_inc(rest_in, 16)
            sp.wait_ge(zeros_ready, 2)
            sp.dma_start(dots[DENSE_Q * SLOT:DENSE_Q * SLOT + ND, :, 0, DENSE_K, :],
                         dense_t.rearrange("n (t b) -> n t b", t=T)).then_inc(dense_in, 16)
            sp.wait_ge(y_ready, 3)
            sp.dma_start(y, y_sb[:, :]).then_inc(y_out, 16)
            sp.wait_ge(y_out, 16)

        @block.gpsimd
        def _(pool):
            nc.gpsimd.iota(row_int[:], pattern=[[1, CH]], base=0, channel_multiplier=CH).then_inc(row_made, 1)
            nc.gpsimd.memset(ident[:], 0.0).then_inc(ident_zero, 1)
            pool.wait_ge(ident_zero, 1)
            nc.gpsimd.affine_select(out=ident[:], in_=ident[:], compare_op=ALU.not_equal, fill=1.0, base=0,
                                    pattern=[[-1, P]], channel_multiplier=1).then_inc(ident_ready, 1)
            pool.wait_ge(ids_in, 16)
            for t in range(T):
                for g, (a, e) in enumerate(TG):
                    for n in range(a, e):
                        f = GATHERED[n]
                        nc.gpsimd.indirect_dma_start(
                            out=emb[:, t, n, :], out_offset=None, in_=tbls[f],
                            in_offset=bass.IndirectOffsetOnAxis(ap=ids_sb[:, t, f:f + 1], axis=0),
                        ).then_inc(gathered[t][g], 16)

        def take_fill(eng, copy, taken, what):
            i = FILL_NO[what]
            eng.wait_ge(filled, i + 1)
            if what[0] == "oh":
                copy(embT[:, :, :, what[1]].rearrange("p t b -> p (t b)"), fill[:, i % 2, :]).then_inc(taken, 1)
            else:
                _, t, g = what
                a, e = TG[g]
                copy(embT_u[:, t, :, X + a:X + e, :], fill_u[:, i % 2, :, 0:e - a, :]).then_inc(taken, 1)

        def take_unit(eng, copy, taken, t, u, samples):
            i = t * UNITS + u
            eng.wait_ge(gram_ready, i + 1)
            for s in samples:
                for q in range(Q):
                    nk = min(K1, MERGED - K1 * q)
                    c = SLOT * s + K1 * q
                    one = gram[i % 2][SLOT * s:SLOT * (s + 1), :, c:c + nk]
                    src = bass.AP(tensor=one.tensor, offset=one.offset, ap=[one.ap[0], one.ap[1], [HALF, 2], one.ap[2]])
                    dst = dots[SLOT * q:SLOT * (q + 1), t, :, 0:nk, u * US:(u + 1) * US].rearrange(
                        "p h k (g s) -> p s g h k", s=GS)[:, s]
                    last = copy(dst, src)
            last.then_inc(taken, 1)

        @block.vector
        def _(dve):
            def make_onehot(n):
                if n >= 2:
                    dve.wait_ge(filled, FILL_NO[("oh", n - 2)] + 1)
                dve.wait_ge(ids16_ready, n + 1)
                for c in range(CH):
                    nc.vector.tensor_scalar(onehot[:, n % 2, c, :], ids_16[:, n, :], row_no[0:CR, c:c + 1], None,
                                            ALU.is_equal).then_inc(onehot_ready, 1)
                dve.wait_ge(table_in[n], 16)
                nc.vector.tensor_tensor(rest[:, n % 2, :].rearrange("p (c d) -> p c d", d=D),
                                        table[:, n % NT, :].rearrange("p (c d) -> p c d", d=D),
                                        table_hi[:, n % NT, :, :], ALU.subtract).then_inc(rest_ready, 1)
                dve.wait_ge(rest_ready, n + 1)
                nc.vector.tensor_tensor(low_c[:, n % 2, :, :],
                                        rest[:, n % 2, :].rearrange("p (c d) -> p c d", d=D),
                                        rest_hi[:, n % 2, :, :], ALU.subtract).then_inc(low_ready, 1)

            def take_tile(t):
                for u in range(UNITS):
                    i = t * UNITS + u
                    take_unit(dve, nc.vector.tensor_copy, dots_v, t, u, (2, 3))
                    dve.wait_ge(dots_v, i + 1)
                    dve.wait_ge(dots_a, i + 1)
                    b = slice(u * US, (u + 1) * US)
                    nc.vector.copy_predicated(dots[:, t, 0, :, b], pick_sb[:].unsqueeze(2).broadcast_to([P, K1, US]),
                                              dots[:, t, 1, :, b]).then_inc(merged, 1)

            def take_fills(t, groups):
                for g in groups:
                    if taker(FILL_NO[("tr", t, g)]) == "dve":
                        take_fill(dve, nc.vector.tensor_copy, taken_v, ("tr", t, g))

            def layers(r, t0, t1, between=()):
                n = (t1 - t0) * P
                dve.wait_ge(layer1_ready, 2 * r + 2)
                for m in (2, 3):
                    nc.vector.tensor_scalar(h1[:, m, 0:n], layer[1][:, (m - 2) * n:(m - 1) * n], b1_sb[:, m:m + 1],
                                            0.0, ALU.add, ALU.max).then_inc(h1_v, 1)
                take_fills(t1, between)
                dve.wait_ge(layer2_ready, 2 * r + 2)
                nc.vector.tensor_scalar(h2[:, 1, 0:n], layer[1][:, 0:n], b2_sb[:, 1:2], 0.0, ALU.add,
                                        ALU.max).then_inc(h2_v, 1)
                dve.wait_ge(layer3_ready, r + 1)
                nc.vector.tensor_copy(y_sb[:, t0 * P:t1 * P], layer[0][0:1, 2 * P:2 * P + n]).then_inc(y_ready, 1)

            nc.vector.memset(embT[:, :, :, F:SLOT].rearrange("p t b s -> p (t b) s"), 0.0).then_inc(zeros_ready, 1)
            dve.wait_ge(row_made, 1)
            nc.vector.tensor_copy(row_no[:], row_int[:]).then_inc(row_ready, 1)
            dve.wait_ge(row_ready, 1)
            for n in range(X):
                make_onehot(n)
                if n == 1:
                    nc.vector.memset(dots[DENSE_Q * SLOT:P, :, :, DENSE_K:K1, :].rearrange(
                        "p t h k b -> p (t h) (k b)"), 0.0).then_inc(zeros_ready, 1)
            dve.wait_ge(rest_in, 48)
            dve.wait_ge(dense_in, 16)
            take_tile(0)
            take_tile(1)
            take_fills(2, range(0, 3))
            layers(0, 0, 2, between=range(3, NTG))
            take_tile(2)
            take_fills(3, range(0, 3))
            layers(1, 2, 3, between=range(3, 4))
            take_fills(3, range(4, NTG))
            take_tile(3)
            layers(2, 3, 4)

        @block.scalar
        def _(act):
            def take_tile(t):
                for u in range(UNITS):
                    take_unit(act, nc.scalar.copy, dots_a, t, u, (0, 1))

            def take_fills(t, groups):
                for g in groups:
                    if taker(FILL_NO[("tr", t, g)]) == "act":
                        take_fill(act, nc.scalar.copy, taken_a, ("tr", t, g))

            def layers(r, t0, t1, between=()):
                n = (t1 - t0) * P
                act.wait_ge(layer1_ready, 2 * r + 1)
                for m in (0, 1):
                    nc.scalar.activation(h1[:, m, 0:n], layer[0][:, m * n:(m + 1) * n], ACT.Relu,
                                         bias=b1_sb[:, m:m + 1]).then_inc(h1_a, 1)
                take_fills(t1, between)
                act.wait_ge(layer2_ready, 2 * r + 1)
                nc.scalar.activation(h2[:, 0, 0:n], layer[0][:, 0:n], ACT.Relu, bias=b2_sb[:, 0:1]).then_inc(h2_a, 1)

            def shorten(n):
                act.wait_ge(idsbc_in[n], 16)
                nc.scalar.copy(ids_16[:, n, :], ids_bc[:, n, :]).then_inc(ids16_ready, 1)

            shorten(0)
            shorten(1)
            for what in EARLY:
                if what[0] == "oh" and what[1] + 2 < X:
                    shorten(what[1] + 2)
                take_fill(act, nc.scalar.copy, taken_a, what)
            act.wait_ge(rest_in, 48)
            act.wait_ge(zeros_ready, 2)
            take_tile(0)
            take_tile(1)
            take_fills(2, range(0, 3))
            layers(0, 0, 2, between=range(3, NTG))
            take_tile(2)
            take_fills(3, range(0, 3))
            layers(1, 2, 3, between=range(3, 4))
            take_fills(3, range(4, NTG))
            take_tile(3)
            layers(2, 3, 4)

        @block.tensor
        def _(pe):
            def bank_free(i):
                if i >= 2:
                    pe.wait_ge(taken_v if taker(i - 2) == "dve" else taken_a, taken_of(i - 2))

            def one_hot(n):
                i = FILL_NO[("oh", n)]
                bank_free(i)
                pe.wait_ge(table_in[n], 16)
                for c in range(CH):
                    pe.wait_ge(onehot_ready, n * CH + c + 1)
                    nc.tensor.matmul(fill[:, i % 2, :], table_hi[:, n % NT, c, :], onehot[:, n % 2, c, :],
                                     start=(c == 0), stop=False)
                pe.wait_ge(rest_ready, n + 1)
                for c in range(CH):
                    nc.tensor.matmul(fill[:, i % 2, :], rest_hi[:, n % 2, c, :], onehot[:, n % 2, c, :],
                                     start=False, stop=False)
                pe.wait_ge(low_ready, n + 1)
                for c in range(CH):
                    last = nc.tensor.matmul(fill[:, i % 2, :], low_c[:, n % 2, c, :], onehot[:, n % 2, c, :],
                                            start=False, stop=(c == CH - 1))
                last.then_inc(filled, 1)

            def transposes(t, g):
                i = FILL_NO[("tr", t, g)]
                bank_free(i)
                a, e = TG[g]
                pe.wait_ge(gathered[t][g], 16 * (e - a))
                for n in range(a, e):
                    for h in range(2):
                        last = nc.tensor.transpose(fill_h[:, i % 2, n - a, h, :], emb_h[:, t, n, h, :], ident[:])
                last.then_inc(filled, 1)

            def products(t):
                last_fill = max(FILL_NO[("tr", t, NTG - 1)], FILL_NO[("oh", X - 1)])
                for i in (last_fill - 1, last_fill):
                    pe.wait_ge(taken_v if taker(i) == "dve" else taken_a, taken_of(i))
                for u in range(UNITS):
                    i = t * UNITS + u
                    if i >= 2:
                        pe.wait_ge(dots_a, i - 1)
                        pe.wait_ge(dots_v, i - 1)
                    for g in range(UNIT):
                        b = (u * UNIT + g) * GS
                        both = embT[:, t, b:b + GS, :].rearrange("p b s -> p (b s)")
                        last = nc.tensor.matmul(gram[i % 2][:, g, :], both, both, start=True, stop=True)
                    last.then_inc(gram_ready, 1)

            def layers(r, t0, t1, between=()):
                n = (t1 - t0) * P
                if r > 0:
                    pe.wait_ge(y_ready, r)
                pe.wait_ge(merged, UNITS * t1)
                for m in range(MC):
                    for k in range(K1):
                        last = nc.tensor.matmul(layer[m // 2][:, m % 2 * n:(m % 2 + 1) * n],
                                                w1_sb[:, k, m * P:(m + 1) * P], dots[:, t0:t1, 0, k, :],
                                                start=(k == 0), stop=(k == K1 - 1))
                    if m % 2 == 1:
                        last.then_inc(layer1_ready, 1)
                for g in between:
                    transposes(t1, g)
                for m2 in range(MC2):
                    for m in range(MC):
                        pe.wait_ge(h1_a if m < 2 else h1_v, 2 * r + 2)
                        if m == 0 and m2 == 1:
                            pe.wait_ge(h1_v, 2 * r + 2)
                        last = nc.tensor.matmul(layer[m2][:, 0:n], w2_sb[:, m, m2 * P:(m2 + 1) * P], h1[:, m, 0:n],
                                                start=(m == 0), stop=(m == MC - 1))
                    last.then_inc(layer2_ready, 1)
                for m2 in range(MC2):
                    pe.wait_ge(h2_a if m2 == 0 else h2_v, r + 1)
                    last = nc.tensor.matmul(layer[0][0:1, 2 * P:2 * P + n], w3_sb[:, m2:m2 + 1], h2[:, m2, 0:n],
                                            start=(m2 == 0), stop=(m2 == MC2 - 1))
                last.then_inc(layer3_ready, 1)

            pe.wait_ge(ident_ready, 1)
            for what in EARLY:
                if what[0] == "oh":
                    one_hot(what[1])
                else:
                    transposes(what[1], what[2])
            pe.wait_ge(zeros_ready, 2)
            products(0)
            products(1)
            for g in range(0, 3):
                transposes(2, g)
            pe.wait_ge(w1_in, 16)
            pe.wait_ge(rest_in, 48)
            layers(0, 0, 2, between=range(3, NTG))
            products(2)
            for g in range(0, 3):
                transposes(3, g)
            layers(1, 2, 3, between=range(3, 4))
            for g in range(4, NTG):
                transposes(3, g)
            products(3)
            layers(2, 3, 4)


def kernel(**inputs):
    import concourse.bacc as bacc
    from concourse.bass_utils import run_bass_kernel_spmd as run

    nc = bacc.Bacc("TRN2", target_bir_lowering=False, num_devices=1)
    arrays = {}

    def give(name, a):
        a = np.ascontiguousarray(a)
        arrays[name] = a
        return nc.dram_tensor(name, a.shape, mybir.dt.from_np(a.dtype), kind="ExternalInput").ap()

    w_top1 = np.asarray(inputs["W_top1"])
    w1 = np.zeros((P, K1, H1), w_top1.dtype)
    pick = np.zeros((P, K1), np.int32)
    for j in range(F):
        c = j if j < HALF else j - HALF
        for i in ((j + r) % F for r in range(1, HALF + 1)):
            hi, lo = max(ORDER[i], ORDER[j]), min(ORDER[i], ORDER[j])
            w1[SLOT * (c // K1) + i, c % K1] = w_top1[hi * (hi - 1) // 2 + lo]
            pick[SLOT * (c // K1) + i, c % K1] = j >= HALF
    w1[DENSE_Q * SLOT:DENSE_Q * SLOT + ND, DENSE_K] = w_top1[F * (F - 1) // 2:]

    ids = give("ids_dram", inputs["ids"])
    ids_t = give("ids_t_dram", np.asarray(inputs["ids"]).T)
    dense_t = give("dense_t_dram", np.asarray(inputs["dense_ctx"]).T)
    tbls = [give(f"tbl_{f}_dram", inputs[f"tbl_{f}"]) for f in range(F)]
    w1 = give("w1_dram", w1)
    w2 = give("w2_dram", inputs["W_top2"])
    columns = [np.asarray(inputs[n]).reshape(-1, P) for n in ("b_top1", "b_top2", "W_top3")]
    cols = give("cols_dram", np.concatenate(columns).T)
    pick = give("pick_dram", pick)
    y = nc.dram_tensor("y_dram", (B, 1), mybir.dt.float32, kind="ExternalOutput").ap()
    tower(nc, ids, ids_t, dense_t, tbls, w1, w2, cols, pick, y.rearrange("b o -> o b"))
    r = run(nc, [arrays], core_ids=[0])
    return r.results[0]["y_dram"]
```

```python
import numpy as np
import concourse.bass as bass
from concourse import mybir
from contextlib import ExitStack

B = 512
F = 27
D = 128
ND = 16
H1, H2 = 512, 256
P = 128
T = B // P
SLOT = 32
GS = P // SLOT
GROUPS = P // GS
UNIT = 8
UNITS = GROUPS // UNIT
GM = (GS - 1) * SLOT + F
US = UNIT * GS
Q = P // SLOT
BANK = 512

HALF = (F - 1) // 2
MERGED = HALF + 1
K1 = -(-MERGED // Q)
DENSE_Q, DENSE_K = Q - 1, MERGED - K1 * (Q - 1)

ROWS_OH = 1000
CH = 8
CR = ROWS_OH // CH
ACT_C = CH - 1
ONEHOT = [4, 5, 6, 10, 14, 18, 22, 23, 24]
X = len(ONEHOT)
NT = 3
GATHERED = [f for f in range(F) if f not in ONEHOT]
NG = len(GATHERED)
ORDER = ONEHOT + GATHERED
TRANS = 4
TG = [(a, min(a + TRANS, NG)) for a in range(0, NG, TRANS)]
NTG = len(TG)
MC = H1 // P
MC2 = H2 // P
LAST = 2
WARM = 11


BETWEEN = [0, 1, 1, 1, 1, 1, 2, 1, 2]
EARLY_TR = sum(BETWEEN)
assert len(BETWEEN) == X


def fill_order():
    groups = [("tr", t, g) for t in range(T) for g in range(NTG)]
    order = []
    for n in range(X):
        order.append(("oh", n))
        order += groups[:BETWEEN[n]]
        groups = groups[BETWEEN[n]:]
    return order + groups


def tower(nc, ids, ids_t, dense_t, tbls, w1, w2, cols, pick, y):
    fp32, f32r, bf16, i32, u16 = (mybir.dt.float32, mybir.dt.float32r, mybir.dt.bfloat16, mybir.dt.int32,
                                  mybir.dt.uint16)
    ALU = mybir.AluOpType
    ACT = mybir.ActivationFunctionType

    FILLS = fill_order()
    FILL_NO = {w: i for i, w in enumerate(FILLS)}
    EARLY = FILLS[:X + EARLY_TR]

    def bank(i):
        return i % 4 if i < len(EARLY) else i % 2

    def before(i):
        return next((j for j in range(i - 1, -1, -1) if bank(j) == bank(i)), None)

    def taker(i):
        return "act" if i < len(EARLY) or i % 2 else "dve"

    def taken_of(i):
        return sum(taker(j) == taker(i) for j in range(i + 1))

    with ExitStack() as ctx:
        def sb(name, shape, dt=fp32):
            return ctx.enter_context(nc.sbuf_tensor(name, shape, dt))

        def pb(name, shape):
            return ctx.enter_context(nc.psum_tensor(name, shape, fp32))

        def sem(name):
            return ctx.enter_context(nc.semaphore(name))

        ids_sb = sb("ids_sb", [P, T, F], i32)
        ids_bc = sb("ids_bc", [CR, NT, B], i32)
        table = sb("table", [CR, NT, CH * D])
        high = sb("high", [CR, 2, CH * D], f32r)
        low = sb("low", [CR, 2, CH * D], f32r)
        onehot = sb("onehot", [CR, 2, CH, B], f32r)
        row_int = sb("row_int", [P, CH], i32)
        row_no = sb("row_no", [P, CH])
        emb = sb("emb", [P, T, NG, D])
        embT = sb("embT", [P, T, P, SLOT])
        ident = sb("ident", [P, P], bf16)
        dots = sb("dots", [P, T, 2, K1, P])
        pick_sb = sb("pick_sb", [P, K1], i32)
        w1_sb = sb("w1_sb", [P, K1, H1])
        w2_sb = sb("w2_sb", [P, MC, H2])
        cols_sb = sb("cols_sb", [P, MC + 2 * MC2])
        b1_sb = cols_sb[:, 0:MC]
        b2_sb = cols_sb[:, MC:MC + MC2]
        w3_sb = cols_sb[:, MC + MC2:MC + 2 * MC2]
        h1 = sb("h1", [P, MC, 2 * P])
        h2 = sb("h2", [P, MC2, 2 * P])
        y_sb = sb("y_sb", [1, B])

        fill = pb("fill", [P, 4, BANK])
        gram = [pb(f"gram{i}", [P, UNIT, P]) for i in range(2)]
        layer = [fill[:, 2 + i, :] for i in range(2)]

        def sums1(r, m, n):
            if r < LAST:
                return layer[m // 2][:, m % 2 * n:(m % 2 + 1) * n]
            return fill[:, m // 2, m % 2 * n:(m % 2 + 1) * n] if m < 3 else gram[1][:, BANK // P, 0:n]

        def sums2(r, m2, n):
            return layer[m2][:, 0:n] if r < LAST else gram[m2][:, 0, 0:n]

        def sums3(r, n):
            return layer[1][0:1, 2 * P:2 * P + n] if r < LAST else gram[0][0:1, BANK // P, 0:n]

        emb_h = emb[:].bitcast(bf16).rearrange("p t n (d h) -> p t n h d", h=2)
        fill_h = fill[:].bitcast(bf16).rearrange("p i (n h b) -> p i n h b", h=2, b=P)
        fill_u = fill[:].bitcast(u16).rearrange("p i (n h b) -> p i b n h", h=2, b=P)
        embT_u = embT[:].bitcast(u16).rearrange("p t b (s h) -> p t b s h", h=2)

        ids_in = sem("ids_in")
        idsbc_in = [sem(f"idsbc_in{n}") for n in range(X)]
        table_in = [sem(f"table_in{n}") for n in range(X)]
        w1_in = sem("w1_in")
        rest_in = sem("rest_in")
        dense_in = sem("dense_in")
        gathered = [[sem(f"gathered{t}_{g}") for g in range(NTG)] for t in range(T)]
        row_made = sem("row_made")
        row_ready = sem("row_ready")
        ident_zero = sem("ident_zero")
        ident_ready = sem("ident_ready")
        zeros_ready = sem("zeros_ready")
        gram_zero = sem("gram_zero")
        dots_zero = sem("dots_zero")
        onehot_v = sem("onehot_v")
        distance_ready = sem("distance_ready")
        onehot_a = sem("onehot_a")
        high_ready = sem("high_ready")
        low_ready = sem("low_ready")
        filled = sem("filled")
        taken_v = sem("taken_v")
        taken_a = sem("taken_a")
        gram_ready = sem("gram_ready")
        dots_a = sem("dots_a")
        dots_v = sem("dots_v")
        merged = sem("merged")
        layer1_ready = sem("layer1_ready")
        h1_a = sem("h1_a")
        h1_v = sem("h1_v")
        layer2_ready = sem("layer2_ready")
        h2_a = sem("h2_a")
        h2_v = sem("h2_v")
        layer3_ready = sem("layer3_ready")
        y_ready = sem("y_ready")
        y_out = sem("y_out")

        block = ctx.enter_context(nc.Block())

        @block.sync
        def _(sp):
            sp.dma_start(ids_sb[:], ids.rearrange("(t p) f -> p t f", p=P)).then_inc(ids_in, 16)
            for n, f in enumerate(ONEHOT):
                if n == NT:
                    sp.dma_start(w1_sb[:], w1).then_inc(w1_in, 16)
                if n >= NT:
                    sp.wait_ge(filled, FILL_NO[("oh", n - NT)] + 1)
                sp.dma_start(ids_bc[:, n % NT, :], ids_t[f:f + 1, :].broadcast_to([CR, B])).then_inc(idsbc_in[n], 16)
                sp.dma_start(table[:, n % NT, :], tbls[f].rearrange("(p c) d -> p (c d)", c=CH)).then_inc(
                    table_in[n], 16)
            sp.dma_start(w2_sb[:], w2.rearrange("(c p) n -> p c n", p=P)).then_inc(rest_in, 16)
            sp.dma_start(cols_sb[:], cols).then_inc(rest_in, 16)
            sp.dma_start(pick_sb[:], pick).then_inc(rest_in, 16)
            sp.wait_ge(dots_zero, 1)
            sp.dma_start(dots[DENSE_Q * SLOT:DENSE_Q * SLOT + ND, :, 0, DENSE_K, :],
                         dense_t.rearrange("n (t b) -> n t b", t=T)).then_inc(dense_in, 16)
            sp.wait_ge(y_ready, 3)
            sp.dma_start(y, y_sb[:, :]).then_inc(y_out, 16)
            sp.wait_ge(y_out, 16)

        @block.gpsimd
        def _(pool):
            nc.gpsimd.iota(row_int[:], pattern=[[1, CH]], base=0, channel_multiplier=CH).then_inc(row_made, 1)
            nc.gpsimd.memset(ident[:], 0.0).then_inc(ident_zero, 1)
            pool.wait_ge(ident_zero, 1)
            nc.gpsimd.affine_select(out=ident[:], in_=ident[:], compare_op=ALU.not_equal, fill=1.0, base=0,
                                    pattern=[[-1, P]], channel_multiplier=1).then_inc(ident_ready, 1)
            pool.wait_ge(ids_in, 16)
            for t in range(T):
                for g, (a, e) in enumerate(TG):
                    for n in range(a, e):
                        f = GATHERED[n]
                        nc.gpsimd.indirect_dma_start(
                            out=emb[:, t, n, :], out_offset=None, in_=tbls[f],
                            in_offset=bass.IndirectOffsetOnAxis(ap=ids_sb[:, t, f:f + 1], axis=0),
                        ).then_inc(gathered[t][g], 16)

        def take_fill(eng, copy, taken, what):
            i = FILL_NO[what]
            eng.wait_ge(filled, i + 1)
            if what[0] == "oh":
                copy(embT[:, :, :, what[1]].rearrange("p t b -> p (t b)"), fill[:, bank(i), :]).then_inc(taken, 1)
            else:
                _, t, g = what
                a, e = TG[g]
                copy(embT_u[:, t, :, X + a:X + e, :], fill_u[:, bank(i), :, 0:e - a, :]).then_inc(taken, 1)

        def take_unit(eng, copy, taken, t, u, samples):
            i = t * UNITS + u
            eng.wait_ge(gram_ready, i + 1)
            for s in samples:
                for q in range(Q):
                    nk = min(K1, MERGED - K1 * q)
                    c = F * s + K1 * q
                    one = gram[i % 2][SLOT * s:SLOT * (s + 1), :, c:c + nk]
                    src = bass.AP(tensor=one.tensor, offset=one.offset, ap=[one.ap[0], one.ap[1], [HALF, 2], one.ap[2]])
                    dst = dots[SLOT * q:SLOT * (q + 1), t, :, 0:nk, u * US:(u + 1) * US].rearrange(
                        "p h k (g s) -> p s g h k", s=GS)[:, s]
                    last = copy(dst, src)
            last.then_inc(taken, 1)

        @block.vector
        def _(dve):
            def make_onehot(n):
                if n >= 2:
                    dve.wait_ge(filled, FILL_NO[("oh", n - 2)] + 1)
                dve.wait_ge(idsbc_in[n], 16)
                for c in range(ACT_C):
                    nc.vector.tensor_scalar(onehot[:, n % 2, c, :], ids_bc[:, n % NT, :], row_no[0:CR, c:c + 1], None,
                                            ALU.is_equal).then_inc(onehot_v, 1)
                dve.wait_ge(high_ready, 2 * n + 2)
                nc.vector.tensor_tensor(low[:, n % 2, :], table[:, n % NT, :], high[:, n % 2, :].bitcast(fp32),
                                        ALU.subtract).then_inc(low_ready, 1)

            def take_transposes(*groups):
                for t, g in groups:
                    if taker(FILL_NO[("tr", t, g)]) == "dve":
                        take_fill(dve, nc.vector.tensor_copy, taken_v, ("tr", t, g))

            def take_products(t, between={}):
                for u in range(UNITS):
                    i = t * UNITS + u
                    take_transposes(*between.get(u, ()))
                    take_unit(dve, nc.vector.tensor_copy, dots_v, t, u, (2, 3))
                    dve.wait_ge(dots_v, i + 1)
                    dve.wait_ge(dots_a, i + 1)
                    b = slice(u * US, (u + 1) * US)
                    nc.vector.copy_predicated(dots[:, t, 0, :, b], pick_sb[:].unsqueeze(2).broadcast_to([P, K1, US]),
                                              dots[:, t, 1, :, b]).then_inc(merged, 1)

            def take_layer1(r, t0, t1):
                n = (t1 - t0) * P
                for m in (2, 3):
                    dve.wait_ge(layer1_ready, 2 * r + (m if r == LAST else 2))
                    nc.vector.tensor_scalar(h1[:, m, 0:n], sums1(r, m, n), b1_sb[:, m:m + 1],
                                            0.0, ALU.add, ALU.max).then_inc(h1_v, 1)

            def take_layer2(r, t0, t1):
                n = (t1 - t0) * P
                dve.wait_ge(layer2_ready, 2 * r + 2)
                nc.vector.tensor_scalar(h2[:, 1, 0:n], sums2(r, 1, n), b2_sb[:, 1:2], 0.0, ALU.add,
                                        ALU.max).then_inc(h2_v, 1)

            def take_layer3(r, t0, t1):
                n = (t1 - t0) * P
                dve.wait_ge(layer3_ready, r + 1)
                nc.vector.tensor_copy(y_sb[:, t0 * P:t1 * P], sums3(r, n)).then_inc(y_ready, 1)

            nc.vector.memset(embT[:, :, :, F:SLOT].rearrange("p t b s -> p (t b) s"), 0.0).then_inc(zeros_ready, 1)
            dve.wait_ge(row_made, 1)
            nc.vector.tensor_copy(row_no[:], row_int[:]).then_inc(row_ready, 1)
            dve.wait_ge(row_ready, 1)
            for n in range(X):
                make_onehot(n)
            dve.wait_ge(rest_in, 48)
            dve.wait_ge(dense_in, 16)
            take_products(0)
            take_products(1, {0: [(2, 0)], 2: [(2, 1)]})
            take_transposes((2, 2), (2, 3))
            take_layer1(0, 0, 2)
            take_transposes((2, 4))
            take_products(2, {1: [(3, 0)], 3: [(3, 1)]})
            take_layer2(0, 0, 2)
            take_layer3(0, 0, 2)
            take_transposes((3, 2), (3, 3), (3, 4))
            take_layer1(1, 2, 3)
            take_products(3)
            take_layer2(1, 2, 3)
            take_layer1(2, 3, 4)
            take_layer3(1, 2, 3)
            take_layer2(2, 3, 4)
            take_layer3(2, 3, 4)

        @block.scalar
        def _(act):
            def take_transposes(*groups):
                for t, g in groups:
                    if taker(FILL_NO[("tr", t, g)]) == "act":
                        take_fill(act, nc.scalar.copy, taken_a, ("tr", t, g))

            def take_products(t, between={}):
                for u in range(UNITS):
                    take_transposes(*between.get(u, ()))
                    take_unit(act, nc.scalar.copy, dots_a, t, u, (0, 1))

            def take_layer1(r, t0, t1):
                n = (t1 - t0) * P
                act.wait_ge(layer1_ready, 2 * r + 1)
                for m in (0, 1):
                    nc.scalar.activation(h1[:, m, 0:n], sums1(r, m, n), ACT.Relu,
                                         bias=b1_sb[:, m:m + 1]).then_inc(h1_a, 1)

            def take_layer2(r, t0, t1):
                n = (t1 - t0) * P
                act.wait_ge(layer2_ready, 2 * r + 1)
                nc.scalar.activation(h2[:, 0, 0:n], sums2(r, 0, n), ACT.Relu, bias=b2_sb[:, 0:1]).then_inc(h2_a, 1)

            def onehot_chunk(n):
                if n >= 2:
                    act.wait_ge(filled, FILL_NO[("oh", n - 2)] + 1)
                act.wait_ge(idsbc_in[n], 16)
                chunk = onehot[:, n % 2, ACT_C, :]
                nc.scalar.activation(chunk, ids_bc[:, n % NT, :], ACT.Abs, bias=row_no[0:CR, ACT_C:ACT_C + 1],
                                     scale=-1.0).then_inc(distance_ready, 1)
                act.wait_ge(distance_ready, n + 1)
                nc.scalar.activation(chunk, chunk.bitcast(fp32), ACT.Relu, bias=1.0, scale=-1.0).then_inc(onehot_a, 1)

            def round_table(n):
                act.wait_ge(table_in[n], 16)
                if n >= 2:
                    act.wait_ge(filled, FILL_NO[("oh", n - 2)] + 1)
                half = CH * D // 2
                for a in (0, half):
                    nc.scalar.copy(high[:, n % 2, a:a + half], table[:, n % NT, a:a + half]).then_inc(high_ready, 1)

            act.wait_ge(ident_ready, 1)
            for i in range(2):
                nc.scalar.mul(gram[i][GM // SLOT * SLOT:P, :, :],
                              ident[GM // SLOT * SLOT:P, :].unsqueeze(1).broadcast_to([SLOT, UNIT, P]),
                              0.0).then_inc(gram_zero, 1)
            act.wait_ge(row_ready, 1)
            onehot_chunk(0)
            round_table(0)
            onehot_chunk(1)
            round_table(1)
            act.wait_ge(zeros_ready, 1)
            nc.scalar.copy(dots[DENSE_Q * SLOT:P, :, :, DENSE_K:K1, :].rearrange("p t h k b -> p (t h) (k b)"),
                           embT[DENSE_Q * SLOT:P, 0, 0:1, F:F + 1].broadcast_to(
                               [SLOT, 2 * T, (K1 - DENSE_K) * P])).then_inc(dots_zero, 1)
            for what in EARLY:
                take_fill(act, nc.scalar.copy, taken_a, what)
                if what[0] == "oh" and what[1] + 2 < X:
                    round_table(what[1] + 2)
                    onehot_chunk(what[1] + 2)
            act.wait_ge(rest_in, 48)
            act.wait_ge(dots_zero, 1)
            take_products(0)
            take_products(1, {0: [(2, 0)], 2: [(2, 1)]})
            take_transposes((2, 2))
            take_layer1(0, 0, 2)
            take_transposes((2, 3), (2, 4))
            take_layer2(0, 0, 2)
            take_products(2, {1: [(3, 0)], 3: [(3, 1)]})
            take_transposes((3, 2))
            take_layer1(1, 2, 3)
            take_transposes((3, 3), (3, 4))
            take_products(3)
            take_layer2(1, 2, 3)
            take_layer1(2, 3, 4)
            take_layer2(2, 3, 4)

        @block.tensor
        def _(pe):
            def bank_free(i):
                j = before(i)
                if j is not None:
                    pe.wait_ge(taken_v if taker(j) == "dve" else taken_a, taken_of(j))

            def one_hot(n):
                i = FILL_NO[("oh", n)]
                bank_free(i)
                for c in range(CH):
                    if c % (CH // 2) == 0:
                        pe.wait_ge(high_ready, 2 * n + 1 + c // (CH // 2))
                    if c == ACT_C:
                        pe.wait_ge(onehot_a, n + 1)
                    else:
                        pe.wait_ge(onehot_v, n * ACT_C + c + 1)
                    nc.tensor.matmul(fill[:, bank(i), :], high[:, n % 2, c * D:(c + 1) * D], onehot[:, n % 2, c, :],
                                     start=(c == 0), stop=False)
                pe.wait_ge(low_ready, n + 1)
                for c in range(CH):
                    last = nc.tensor.matmul(fill[:, bank(i), :], low[:, n % 2, c * D:(c + 1) * D],
                                            onehot[:, n % 2, c, :], start=False, stop=(c == CH - 1))
                last.then_inc(filled, 1)

            def transposes(*groups):
                for t, g in groups:
                    i = FILL_NO[("tr", t, g)]
                    bank_free(i)
                    a, e = TG[g]
                    pe.wait_ge(gathered[t][g], 16 * (e - a))
                    for n in range(a, e):
                        for h in range(2):
                            last = nc.tensor.transpose(fill_h[:, bank(i), n - a, h, :], emb_h[:, t, n, h, :],
                                                       ident[:])
                    last.then_inc(filled, 1)

            def products(t, between={}):
                last_fill = max(FILL_NO[("tr", t, NTG - 1)], FILL_NO[("oh", X - 1)])
                for i in (last_fill - 1, last_fill):
                    pe.wait_ge(taken_v if taker(i) == "dve" else taken_a, taken_of(i))
                for u in range(UNITS):
                    i = t * UNITS + u
                    transposes(*between.get(u, ()))
                    if i >= 2:
                        pe.wait_ge(dots_a, i - 1)
                        pe.wait_ge(dots_v, i - 1)
                    for g in range(UNIT):
                        b = (u * UNIT + g) * GS
                        last = nc.tensor.matmul(gram[i % 2][0:GM, g, 0:GS * F],
                                                embT[:, t, b:b + GS, :].rearrange("p b s -> p (b s)")[:, 0:GM],
                                                embT[:, t, b:b + GS, 0:F], start=True, stop=True)
                    last.then_inc(gram_ready, 1)

            def layer1_part(r, m, t0, t1, a, e):
                pe.wait_ge(merged, UNITS * e)
                for k in range(K1):
                    last = nc.tensor.matmul(sums1(r, m, (t1 - t0) * P)[:, (a - t0) * P:(e - t0) * P],
                                            w1_sb[:, k, m * P:(m + 1) * P], dots[:, a:e, 0, k, :],
                                            start=(k == 0), stop=(k == K1 - 1))
                return last

            def layer1(r, t0, t1, after_m1=(), after_m2=()):
                for t in range(t0, t1):
                    for m in (0, 1):
                        last = layer1_part(r, m, t0, t1, t, t + 1)
                last.then_inc(layer1_ready, 1)
                transposes(*after_m1)
                if 0 < r < LAST:
                    pe.wait_ge(y_ready, r)
                last = layer1_part(r, 2, t0, t1, t0, t1)
                if r == LAST:
                    last.then_inc(layer1_ready, 1)
                transposes(*after_m2)
                layer1_part(r, 3, t0, t1, t0, t1).then_inc(layer1_ready, 1)

            def layer2_part(r, t0, t1, m2, ms):
                n = (t1 - t0) * P
                for m in ms:
                    pe.wait_ge(h1_a if m < 2 else h1_v, 2 * r + m % 2 + 1)
                    last = nc.tensor.matmul(sums2(r, m2, n), w2_sb[:, m, m2 * P:(m2 + 1) * P], h1[:, m, 0:n],
                                            start=(m == 0), stop=(m == MC - 1))
                return last

            def layer2(r, t0, t1, m2):
                pe.wait_ge(h1_a, 2 * r + 2)
                if m2 == 1:
                    pe.wait_ge(h1_v, 2 * r + 2)
                layer2_part(r, t0, t1, m2, range(MC)).then_inc(layer2_ready, 1)

            def layer3(r, t0, t1):
                n = (t1 - t0) * P
                if r < LAST:
                    pe.wait_ge(h2_v, r + 1)
                for m2 in range(MC2):
                    pe.wait_ge(h2_a if m2 == 0 else h2_v, r + 1)
                    last = nc.tensor.matmul(sums3(r, n), w3_sb[:, m2:m2 + 1], h2[:, m2, 0:n],
                                            start=(m2 == 0), stop=(m2 == MC2 - 1))
                last.then_inc(layer3_ready, 1)

            pe.wait_ge(ident_ready, 1)
            for _ in range(WARM):
                nc.tensor.matmul(fill[:, 3, :].rearrange("p (r c) -> p r c", r=4), ident[:],
                                 ident[:].unsqueeze(1).broadcast_to([P, 4, P]), start=True, stop=True)
            for what in EARLY:
                if what[0] == "oh":
                    one_hot(what[1])
                else:
                    transposes(what[1:])
            pe.wait_ge(zeros_ready, 1)
            pe.wait_ge(gram_zero, 2)
            pe.wait_ge(dots_zero, 1)
            products(0)
            products(1, {0: [(2, 0)], 2: [(2, 1)]})
            transposes((2, 2))
            pe.wait_ge(w1_in, 16)
            pe.wait_ge(rest_in, 48)
            layer1(0, 0, 2, after_m2=[(2, 3)])
            transposes((2, 4))
            layer2(0, 0, 2, 0)
            products(2, {1: [(3, 0)], 3: [(3, 1)]})
            layer2(0, 0, 2, 1)
            transposes((3, 2))
            layer3(0, 0, 2)
            layer1(1, 2, 3, after_m1=[(3, 3)], after_m2=[(3, 4)])
            products(3)
            layer2(1, 2, 3, 0)
            layer2(1, 2, 3, 1)
            layer1(2, 3, 4)
            layer3(1, 2, 3)
            for ms in ((0, 1), (2, 3)):
                for m2 in range(MC2):
                    last = layer2_part(2, 3, 4, m2, ms)
                    if ms[-1] == MC - 1:
                        last.then_inc(layer2_ready, 1)
            layer3(2, 3, 4)


def kernel(**inputs):
    import concourse.bacc as bacc
    from concourse.bass_utils import run_bass_kernel_spmd as run

    nc = bacc.Bacc("TRN2", target_bir_lowering=False, num_devices=1)
    arrays = {}

    def give(name, a):
        a = np.ascontiguousarray(a)
        arrays[name] = a
        return nc.dram_tensor(name, a.shape, mybir.dt.from_np(a.dtype), kind="ExternalInput").ap()

    w_top1 = np.asarray(inputs["W_top1"])
    w1 = np.zeros((P, K1, H1), w_top1.dtype)
    pick = np.zeros((P, K1), np.int32)
    for j in range(F):
        c = j if j < HALF else j - HALF
        for i in ((j + r) % F for r in range(1, HALF + 1)):
            hi, lo = max(ORDER[i], ORDER[j]), min(ORDER[i], ORDER[j])
            w1[SLOT * (c // K1) + i, c % K1] = w_top1[hi * (hi - 1) // 2 + lo]
            pick[SLOT * (c // K1) + i, c % K1] = j >= HALF
    w1[DENSE_Q * SLOT:DENSE_Q * SLOT + ND, DENSE_K] = w_top1[F * (F - 1) // 2:]

    ids = give("ids_dram", inputs["ids"])
    ids_t = give("ids_t_dram", np.asarray(inputs["ids"]).T)
    dense_t = give("dense_t_dram", np.asarray(inputs["dense_ctx"]).T)
    tbls = [give(f"tbl_{f}_dram", inputs[f"tbl_{f}"]) for f in range(F)]
    w1 = give("w1_dram", w1)
    w2 = give("w2_dram", inputs["W_top2"])
    columns = [np.asarray(inputs[n]).reshape(-1, P) for n in ("b_top1", "b_top2", "W_top3")]
    cols = give("cols_dram", np.concatenate(columns).T)
    pick = give("pick_dram", pick)
    y = nc.dram_tensor("y_dram", (B, 1), mybir.dt.float32, kind="ExternalOutput").ap()
    tower(nc, ids, ids_t, dense_t, tbls, w1, w2, cols, pick, y.rearrange("b o -> o b"))
    r = run(nc, [arrays], core_ids=[0])
    return r.results[0]["y_dram"]
```
